# Optimizing a Trainium2 kernel written in Bass

```python
import numpy as np
import jax
import jax.numpy as jnp

def _softmax(x, axis=-1):
    return jax.nn.softmax(x, axis=axis)
def _gelu(x):
    return jax.nn.gelu(x, approximate=True)
def _silu(x):
    return jax.nn.silu(x)
def _sigmoid(x):
    return jax.nn.sigmoid(x)
def _layernorm(x, axis=-1, eps=1e-5):
    m = jnp.mean(x, axis=axis, keepdims=True)
    v = jnp.var(x, axis=axis, keepdims=True)
    return (x - m) / jnp.sqrt(v + eps)
def _scatter_add(tgt, idx, src, axis=0):
    return tgt.at[idx].add(src)
def _segment_sum(src, seg, n):
    return jax.ops.segment_sum(src, seg, n)

kernel_name = 'mk_conv_preact_d2_conv_nhwc192_fe9032'

def setup_inputs(seed: int = 0):
    np.random.seed(seed)
    _w = jnp.asarray
    def _rec_inputs():
        import jax
        import jax.numpy as jnp
        _gk = jax.random.key(seed)
        x = -0.0003482 + 1 * jax.random.normal(jax.random.fold_in(_gk, 1), (4, 128, 192, 192), jnp.float32)
        return x
    x = _rec_inputs()
    def _L0_conv_setup():
        import jax, jax.numpy as jnp
        import numpy as np
        K_SIZE = 7
        key = jax.random.key(seed)
        k0, k1, k2, k3 = jax.random.split(key, 4)
        B, C, H, W = (4, 128, 192, 192)
        O, K = (128, K_SIZE)
        x = jax.random.normal(k0, (B, C, H, W), dtype=jnp.float32)
        offsets = jax.random.normal(k1, (B, K, H, W), dtype=jnp.float32) * 0.5
        tumor_center = jax.random.uniform(k2, (B, 2), dtype=jnp.float32) * H
        kernel_w = jax.random.normal(k3, (O * K, C), dtype=jnp.float32) / np.sqrt(C)
        kernel_b = jnp.zeros((O * K,), dtype=jnp.float32)
        return {'x': x, 'offsets': offsets, 'tumor_center': tumor_center, 'kernel_w': kernel_w, 'kernel_b': kernel_b}
    _L0_conv_all = _L0_conv_setup()
    _L0_conv_in = {k: v for k, v in _L0_conv_all.items() if k in ('offsets', 'tumor_center', 'kernel_w', 'kernel_b', )}
    del _L0_conv_all

    def _L1_conv_setup():
        import jax, jax.numpy as jnp
        import numpy as np
        K_SIZE = 7
        key = jax.random.key(seed)
        k0, k1, k2, k3 = jax.random.split(key, 4)
        B, C, H, W = (4, 128, 192, 192)
        O, K = (128, K_SIZE)
        x = jax.random.normal(k0, (B, C, H, W), dtype=jnp.float32)
        offsets = jax.random.normal(k1, (B, K, H, W), dtype=jnp.float32) * 0.5
        tumor_center = jax.random.uniform(k2, (B, 2), dtype=jnp.float32) * H
        kernel_w = jax.random.normal(k3, (O * K, C), dtype=jnp.float32) / np.sqrt(C)
        kernel_b = jnp.zeros((O * K,), dtype=jnp.float32)
        return {'x': x, 'offsets': offsets, 'tumor_center': tumor_center, 'kernel_w': kernel_w, 'kernel_b': kernel_b}
    _L1_conv_all = _L1_conv_setup()
    _L1_conv_in = {k: v for k, v in _L1_conv_all.items() if k in ('offsets', 'tumor_center', 'kernel_w', 'kernel_b', )}
    del _L1_conv_all

    return {
        "x": x,
        "L0_conv_offsets": _L0_conv_in["offsets"],
        "L0_conv_tumor_center": _L0_conv_in["tumor_center"],
        "L0_conv_kernel_w": _L0_conv_in["kernel_w"],
        "L0_conv_kernel_b": _L0_conv_in["kernel_b"],
        "L1_conv_offsets": _L1_conv_in["offsets"],
        "L1_conv_tumor_center": _L1_conv_in["tumor_center"],
        "L1_conv_kernel_w": _L1_conv_in["kernel_w"],
        "L1_conv_kernel_b": _L1_conv_in["kernel_b"],
    }

def reference(x, L0_conv_offsets, L0_conv_tumor_center, L0_conv_kernel_w, L0_conv_kernel_b, L1_conv_offsets, L1_conv_tumor_center, L1_conv_kernel_w, L1_conv_kernel_b):
    import jax
    import jax.numpy as jnp
    def _L0_conv_ref(x, offsets, tumor_center, kernel_w, kernel_b):
        import jax, jax.numpy as jnp
        import numpy as np
        K_SIZE = 7
        B, C, H, W = x.shape
        K = K_SIZE
        O = kernel_w.shape[0] // K
        pad = K // 2
        dt = x.dtype
        h_c = tumor_center[:, 0][:, None, None]
        w_c = tumor_center[:, 1][:, None, None]
        h_idx = jnp.arange(H, dtype=dt)[None, :, None]
        w_idx = jnp.arange(W, dtype=dt)[None, None, :]
        dh = h_idx - h_c
        dw = w_idx - w_c
        rnorm = jnp.sqrt(dh * dh + dw * dw + 1e-06)
        dir_h = dh / rnorm
        dir_w = dw / rnorm
        base = jnp.linspace(-pad, pad, K, dtype=dt).reshape(1, K, 1, 1)
        h_grid = base * dir_h[:, None] + offsets
        w_grid = base * dir_w[:, None] + offsets
        h_grid = h_grid / (H - 1) * 2
        w_grid = w_grid / (W - 1) * 2
        grid = jnp.stack([w_grid, h_grid], axis=-1)
        del grid
        kern = jnp.einsum('bchw,fc->bfhw', x, kernel_w) + kernel_b[None, :, None, None]
        kern = kern.reshape(B, O, K, H, W)
        out = jnp.einsum('bchw,bokhw->bohw', x, kern)
        return out

    def _L1_conv_ref(x, offsets, tumor_center, kernel_w, kernel_b):
        import jax, jax.numpy as jnp
        import numpy as np
        K_SIZE = 7
        B, C, H, W = x.shape
        K = K_SIZE
        O = kernel_w.shape[0] // K
        pad = K // 2
        dt = x.dtype
        h_c = tumor_center[:, 0][:, None, None]
        w_c = tumor_center[:, 1][:, None, None]
        h_idx = jnp.arange(H, dtype=dt)[None, :, None]
        w_idx = jnp.arange(W, dtype=dt)[None, None, :]
        dh = h_idx - h_c
        dw = w_idx - w_c
        rnorm = jnp.sqrt(dh * dh + dw * dw + 1e-06)
        dir_h = dh / rnorm
        dir_w = dw / rnorm
        base = jnp.linspace(-pad, pad, K, dtype=dt).reshape(1, K, 1, 1)
        h_grid = base * dir_h[:, None] + offsets
        w_grid = base * dir_w[:, None] + offsets
        h_grid = h_grid / (H - 1) * 2
        w_grid = w_grid / (W - 1) * 2
        grid = jnp.stack([w_grid, h_grid], axis=-1)
        del grid
        kern = jnp.einsum('bchw,fc->bfhw', x, kernel_w) + kernel_b[None, :, None, None]
        kern = kern.reshape(B, O, K, H, W)
        out = jnp.einsum('bchw,bokhw->bohw', x, kern)
        return out

    def _gn(v, G=32, eps=1e-5):
        B_, H_, W_, C_ = v.shape
        g = v.reshape(B_, H_, W_, G, C_ // G)
        m = jnp.mean(g, axis=(1, 2, 4), keepdims=True)
        s = jnp.var(g, axis=(1, 2, 4), keepdims=True)
        return ((g - m) / jnp.sqrt(s + eps)).reshape(v.shape)

    def _ln_c(v, eps=1e-6):
        m = jnp.mean(v, axis=-1, keepdims=True)
        s = jnp.var(v, axis=-1, keepdims=True)
        return (v - m) / jnp.sqrt(s + eps)

    def _ln_t(v, eps=1e-5):
        m = jnp.mean(v, axis=-1, keepdims=True)
        s = jnp.var(v, axis=-1, keepdims=True)
        return (v - m) / jnp.sqrt(s + eps)

    def _to_tokens(v):
        B_, H_, W_, C_ = v.shape
        return v.reshape(B_, H_ * W_, C_)
    def _from_tokens(t, like):
        return t.reshape(like.shape)

    x = x + _L0_conv_ref(_gn(x), L0_conv_offsets, L0_conv_tumor_center, L0_conv_kernel_w, L0_conv_kernel_b)
    x = x + _L1_conv_ref(_gn(x), L1_conv_offsets, L1_conv_tumor_center, L1_conv_kernel_w, L1_conv_kernel_b)
    return x


_drawn_inputs = setup_inputs


def setup_inputs(seed=0):
    import zlib

    import numpy as np

    out = dict(_drawn_inputs(seed))
    spreads = {'L0_conv_kernel_b': (0.0, 0.1), 'L1_conv_kernel_b': (0.0, 0.1)}
    factors = {}
    for name, (base, spread) in spreads.items():
        noise = np.random.default_rng([zlib.crc32(name.encode()), seed]).standard_normal(out[name].shape)
        drawn = base * np.exp(spread * noise) if base else spread * noise
        out[name] = jnp.asarray(drawn.astype(out[name].dtype))
    for name, factor in factors.items():
        out[name] = (out[name] * factor).astype(out[name].dtype)
    return out
```

```python
from contextlib import ExitStack

import concourse.bass as bass
from concourse import mybir

F32 = mybir.dt.float32
F32R = mybir.dt.float32r
BF16 = mybir.dt.bfloat16
ALU = mybir.AluOpType
ACT = mybir.ActivationFunctionType
AX = mybir.AxisListType

C = 128
TAPS = 7
GROUPS = 32
EPS = 1e-5
QUARTERS = 4
SLOTS = 5
OCTET = 8
LAYERS = 2


def build(nc, x, w0, b0, w1, b1, out):
    B, _, H, W = x.shape
    ROWS = H // QUARTERS
    GW = W // GROUPS
    PIX = ROWS * GW
    PW = 2 * GW
    COUNT = C * H * GW
    HALF = PIX // 2
    OCTETS = GROUPS // OCTET
    STEPS0 = OCTET
    STEPS1 = OCTET // 2
    STEPS = OCTETS * (STEPS0 + 2 * STEPS1)
    assert PIX <= 512 and (PIX % 2, H % QUARTERS, W % GROUPS) == (0, 0, 0)

    slots, frees, spare = [list(range(QUARTERS))], [], SLOTS - 1
    for b in range(B):
        now = slots[-1]
        upper = sorted((0, 1), key=lambda q: abs(now[q] - spare))
        third = now[upper[1]]
        lower = sorted((2, 3), key=lambda q: abs(now[q] - third))
        frees.append(upper + lower)
        slots.append([spare, now[upper[0]], third, now[lower[0]]])
        spare = now[lower[1]]

    def slot(b, q):
        return slots[b][q]

    class Step:

        def __init__(s, b, layer, half, octet, k):
            s.b, s.layer, s.octet, s.k = b, layer, octet, k
            if layer == 0:
                s.half, pair = k % 2, k // 2
                s.t = STEPS * b + STEPS0 * octet + k
            else:
                s.half, pair = half, k
                s.t = STEPS * b + OCTETS * STEPS0 + OCTETS * STEPS1 * half + STEPS1 * octet + k
            s.buf = k % 2
            s.group = OCTET * octet + 2 * pair
            s.pair = pair
            low, high = sorted((slot(b, 2 * s.half), slot(b, 2 * s.half + 1)))
            s.quarters = slice(low, high + 1, high - low)

    def steps(b, layer, half, octet):
        return [Step(b, layer, half, octet, k) for k in range(STEPS1 if layer else STEPS0)]

    ctx = ExitStack()
    with ctx:
        def sb(name, shape, dt=F32):
            return ctx.enter_context(nc.sbuf_tensor(name, shape, dt))

        def sem(name):
            return ctx.enter_context(nc.semaphore(name))

        ring = sb("ring", [C, SLOTS, ROWS, W])
        x_hi = sb("x_hi", [C, 2, 2, ROWS, PW], F32R)
        x_lo = sb("x_lo", [C, 2, 2, ROWS, PW], F32R)
        s_sb = sb("s_sb", [C, 2, 2, PIX])
        squares = sb("squares", [C, 2, 2 * PIX], BF16)
        bn_first = sb("bn_first", [C, GROUPS, 6])
        bn_rest = sb("bn_rest", [C, OCTET, QUARTERS - 1, 6])
        mean_sq = sb("mean_sq", [C, OCTET, 2 * QUARTERS])
        sq_sum = sb("sq_sum", [C, OCTET, 2 * QUARTERS])
        parts = [sb(f"parts{l}", [C, 2, GROUPS]) for l in range(LAYERS)]
        y_sum = sb("y_sum", [C, 2, GROUPS])
        x2_sum = sb("x2_sum", [C, 2, GROUPS])
        mean = sb("mean", [C, LAYERS, OCTET])
        ex2 = sb("ex2", [C, LAYERS, OCTET])
        var = sb("var", [C, LAYERS, OCTET])
        std = sb("std", [C, LAYERS, OCTET])
        tmp = sb("tmp", [C, LAYERS, OCTET])
        point5 = sb("point5", [C, OCTET])
        inv_var = sb("inv_var", [C, LAYERS, GROUPS])
        s_bias = sb("s_bias", [C, LAYERS, GROUPS])
        beta = sb("beta", [C, LAYERS, GROUPS])
        wt_hi = sb("wt_hi", [C, LAYERS, C], F32R)
        wt_lo = sb("wt_lo", [C, LAYERS, C], F32R)
        ones = sb("ones", [C, C], F32R)
        w_row = sb("w_row", [C, LAYERS])
        b_sum = sb("b_sum", [C, LAYERS])
        b_in = sb("b_in", [C, LAYERS, TAPS])
        s_ps = ctx.enter_context(nc.psum_tensor("s_ps", [C, 2, 2, 512], F32))
        z_ps = ctx.enter_context(nc.psum_tensor("z_ps", [C, 2, 2, 512], F32))
        stat_ps = z_ps[:, 0, 0, PIX:PIX + 2 * OCTET]

        prep = ring[:, QUARTERS].rearrange("p h w -> p (h w)")
        w_in = prep[:, 0:LAYERS * TAPS * C].rearrange("p (l n) -> p l n", l=LAYERS)
        w_sum = prep[:, LAYERS * TAPS * C:LAYERS * (TAPS + 1) * C].rearrange("p (l n) -> p l n", l=LAYERS)
        ident = prep[:, LAYERS * (TAPS + 1) * C:LAYERS * (TAPS + 1) * C + C]

        loaded = [sem(f"loaded{q}") for q in range(QUARTERS)]
        stored = [sem(f"stored{q}") for q in range(QUARTERS)]
        waited = sem("waited")
        w_loaded = sem("w_loaded")
        ident_ready = sem("ident_ready")
        ones_ready = sem("ones_ready")
        w_summed = sem("w_summed")
        w_turned = sem("w_turned")
        w_hi_ready = sem("w_hi_ready")
        w_ready = sem("w_ready")
        half_ready = sem("half_ready")
        hi_ready = sem("hi_ready")
        lo_ready = sem("lo_ready")
        sums_ready = sem("sums_ready")
        s_ready = sem("s_ready")
        prod_ready = sem("prod_ready")
        y_ready = sem("y_ready")
        added = sem("added")
        squared = sem("squared")
        bn_done = sem("bn_done")
        chain = [sem(f"chain{l}") for l in range(LAYERS)]
        parts_ready = [sem(f"parts_ready{l}") for l in range(LAYERS)]
        stat_ready = [sem(f"stat_ready{l}") for l in range(LAYERS)]
        stat_read = [sem(f"stat_read{l}") for l in range(LAYERS)]
        var_ready = [sem(f"var_ready{l}") for l in range(LAYERS)]
        std_ready = [sem(f"std_ready{l}") for l in range(LAYERS)]
        coef_ready = [sem(f"coef_ready{l}") for l in range(LAYERS)]
        beta_ready = [sem(f"beta_ready{l}") for l in range(LAYERS)]

        def wait(e, s, value):
            if not (isinstance(value, int) and value <= 0):
                e.wait_ge(s, value)

        def columns(st, width, a=0):
            return ring[:, st.quarters, :, bass.ds(GW * st.group + GW * a, width)]

        def octets_of(b, o):
            return OCTETS * b + o

        def finishes(layer, half, o):
            if layer == 0:
                return ([(1, -1, 4)] if o != 0 else []) + ([(0, 1, 6)] if o != OCTETS - 1 else [])
            return [(1, -1, 2)] if (half, o) == (0, 0) else []

        def sections(e, b, emit):
            before = steps(b - 1, 1, 1, OCTETS - 1)[-2:] if b else [None, None]
            for layer, half in ((0, 0), (1, 0), (1, 1)):
                emit(layer, half, 0, 0, before)
                last = OCTETS - 1 if layer == 0 else OCTETS
                with e.Fori(1, last) as octet:
                    emit(layer, half, None, octet, steps(b, layer, half, octet - 1)[-2:])
                if layer == 0:
                    emit(layer, half, last, last, steps(b, layer, half, last - 1)[-2:])
                before = steps(b, layer, half, OCTETS - 1)[-2:]

        block = ctx.enter_context(nc.Block())

        @block.sync
        def _(sp):
            def load(b, q):
                sp.dma_start(ring[:, slot(b, q)], x[b, :, ROWS * q:ROWS * (q + 1)]).then_inc(loaded[q], 16)

            def store(b, q):
                sp.dma_start(out[b, :, ROWS * q:ROWS * (q + 1)], ring[:, slot(b, q)]).then_inc(stored[q], 16)

            sp.dma_start(w_in[:, 0], w0.rearrange("(o k) c -> o (k c)", k=TAPS)).then_inc(w_loaded, 16)
            sp.dma_start(w_in[:, 1], w1.rearrange("(o k) c -> o (k c)", k=TAPS)).then_inc(w_loaded, 16)
            sp.dma_start(b_in[:, 0], b0.rearrange("(o k) -> o k", k=TAPS)).then_inc(w_loaded, 16)
            sp.dma_start(b_in[:, 1], b1.rearrange("(o k) -> o k", k=TAPS)).then_inc(w_loaded, 16)
            for q in range(QUARTERS):
                load(0, q)
            sp.wait_ge(added, 4)
            load(1, 0)
            for b in range(B):
                for half in range(2):
                    sp.wait_ge(added, 2 * (STEPS * b + OCTETS * STEPS0 + OCTETS * STEPS1 * (half + 1)))
                    for i in (2 * half, 2 * half + 1):
                        q = frees[b][i]
                        store(b, q)
                        n = b + 1 + (i + 1) // QUARTERS
                        if n < B:
                            sp.wait_ge(stored[q], 16 * (b + 1))
                            load(n, (i + 1) % QUARTERS)
            for q in range(QUARTERS):
                sp.wait_ge(stored[q], 16 * B)

        @block.scalar
        def _(act):
            for l in range(LAYERS):
                act.wait_ge(w_turned, l + 1)
                nc.scalar.activation(wt_hi[:, l], z_ps[:, l, 0, 0:C], ACT.Copy).then_inc(w_hi_ready, 1)

            def split_hi(st):
                if st.layer == 0:
                    if isinstance(st.octet, int) and st.octet == 0 and st.k < 2:
                        for q in (2 * st.half, 2 * st.half + 1):
                            act.wait_ge(loaded[q], 16 * (st.b + 1))
                else:
                    first = Step(st.b, 0, 0, st.octet, 2 * st.pair + st.half)
                    act.wait_ge(added, 2 * first.t + 2)
                wait(act, prod_ready, 2 * st.t - 2)
                nc.scalar.activation(x_hi[:, st.buf], columns(st, PW), ACT.Copy).then_inc(hi_ready, 1)

            def scale_sums(st, in_loop=False):
                act.wait_ge(coef_ready[st.layer], octets_of(st.b, st.octet) + 1)
                for a in range(2):
                    act.wait_ge(sums_ready, 2 * st.t + a + 1)
                    wait(act, y_ready, 2 * st.t + a - 1)
                    if in_loop:
                        act.sem_inc(waited, 1)
                    g = bass.ds(st.group + a, 1)
                    nc.scalar.activation(s_sb[:, a], s_ps[:, a, :, 0:PIX], ACT.Identity,
                                         scale=inv_var[:, st.layer, g], bias=s_bias[:, st.layer, g]
                                         ).then_inc(s_ready, 1)

            def square(st):
                for a in range(2):
                    act.wait_ge(added, 2 * st.t + a + 1)
                    done = 2 * STEPS0 * octets_of(st.b, st.octet) + 2 * st.k + a
                    wait(act, squared, done - 1)
                    nc.scalar.activation(squares[:, a].rearrange("p (q h w) -> p q h w", q=2, h=ROWS), columns(st, GW, a),
                                         ACT.Square,
                                         accum_out=x2_sum[:, st.half, bass.ds(st.group + a, 1)]).then_inc(squared, 1)

            def section(layer, half, o, octet, before):
                b = image
                line = before + steps(b, layer, half, octet)
                for two, one, st in zip(line, line[1:], line[2:]):
                    split_hi(st)
                    if one is not None:
                        scale_sums(one, in_loop=o is None)
                    if two is not None and two.layer == 0:
                        square(two)

            for image in range(B):
                sections(act, image, section)
            scale_sums(steps(B - 1, 1, 1, OCTETS - 1)[-1])

        @block.gpsimd
        def _(pool):
            nc.gpsimd.memset(ident, 0.0).then_inc(ident_ready, 1)
            pool.wait_ge(ident_ready, 1)
            nc.gpsimd.affine_select(out=ident, in_=ident, compare_op=ALU.not_equal, fill=1.0, base=0,
                                    pattern=[[-1, C]], channel_multiplier=1).then_inc(ident_ready, 1)
            nc.gpsimd.memset(point5[:], 0.5).then_inc(half_ready, 1)
            pool.wait_ge(half_ready, 1)

            def split_lo(st):
                pool.wait_ge(hi_ready, st.t + 1)
                wait(pool, prod_ready, 2 * st.t - 2)
                nc.gpsimd.tensor_tensor(x_lo[:, st.buf], columns(st, PW), x_hi[:, st.buf].bitcast(F32),
                                        ALU.subtract).then_inc(lo_ready, 1)

            def root(l, n):
                pool.wait_ge(var_ready[l], n + 1)
                nc.gpsimd.tensor_tensor(std[:, l], var[:, l], point5[:], ALU.pow).then_inc(std_ready[l], 1)

            def section(layer, half, o, octet, before):
                b = image
                for st in steps(b, layer, half, octet):
                    if (layer, o, st.k) == (0, 0, 1):
                        root(0, octets_of(b, 0))
                    for l, rel, k in finishes(layer, half, o):
                        if st.k == min(k + 1, 3 if layer else 7):
                            root(l, octets_of(b, octet + rel) if layer == 0 else octets_of(b, OCTETS - 1))
                    split_lo(st)

            for image in range(B):
                sections(pool, image, section)

        @block.tensor
        def _(pe):
            pe.wait_ge(w_summed, 1)
            pe.wait_ge(ident_ready, 2)
            for l in range(LAYERS):
                nc.tensor.transpose(z_ps[:, l, 0, 0:C], w_sum[:, l], ident).then_inc(w_turned, 1)
            pe.wait_ge(w_ready, LAYERS)
            pe.wait_ge(ones_ready, 1)

            def add_channels(l, octet, n):
                pe.wait_ge(parts_ready[l], n + 1)
                nc.tensor.matmul(stat_ps.rearrange("p (j g) -> p j g", j=2), ones[:].bitcast(F32),
                                 parts[l][:, :, bass.ds(OCTET * octet, OCTET)], start=True, stop=True
                                 ).then_inc(stat_ready[l], 1)
                pe.wait_ge(stat_read[l], n + 1)

            def sums(st):
                pe.wait_ge(lo_ready, st.t + 1)
                for a in range(2):
                    wait(pe, s_ready, 2 * st.t + a - 1)
                    for q in range(2):
                        for part, x_part in enumerate((x_hi, x_lo)):
                            mm = nc.tensor.matmul(s_ps[:, a, q, 0:PIX], ones[:],
                                                  x_part[:, st.buf, q, :, GW * a:GW * (a + 1)],
                                                  start=(part == 0), stop=(part == 1))
                    mm.then_inc(sums_ready, 1)

            def products(st):
                for a in range(2):
                    wait(pe, added, 2 * st.t + a - 1)
                    for n, (wt, x_part) in enumerate(((wt_hi, x_hi), (wt_hi, x_lo), (wt_lo, x_hi))):
                        for q in range(2):
                            mm = nc.tensor.matmul(z_ps[:, a, q, 0:PIX], wt[:, st.layer],
                                                  x_part[:, st.buf, q, :, GW * a:GW * (a + 1)],
                                                  start=(n == 0), stop=(n == 2))
                    mm.then_inc(prod_ready, 1)

            def section(layer, half, o, octet, before):
                b = image
                for st in steps(b, layer, half, octet):
                    sums(st)
                    if (layer, o, st.k) == (0, 0, 0):
                        wait(pe, added, 2 * st.t - 1)
                        add_channels(0, 0, octets_of(b, 0))
                    for l, rel, k in finishes(layer, half, o):
                        if st.k == k:
                            pe.wait_ge(added, 2 * st.t - 1)
                            of = octet + rel if layer == 0 else OCTETS - 1
                            add_channels(l, of, octets_of(b, of))
                    products(st)

            for image in range(B):
                sections(pe, image, section)

        @block.vector
        def _(dve):
            nc.vector.memset(ones[:].bitcast(F32), 1.0).then_inc(ones_ready, 1)
            dve.wait_ge(w_loaded, 64)
            for l in range(LAYERS):
                nc.vector.tensor_reduce(w_sum[:, l], w_in[:, l].rearrange("p (k c) -> p c k", k=TAPS), AX.X, ALU.add)
            nc.vector.tensor_reduce(b_sum[:], b_in[:], AX.X, ALU.add).then_inc(w_summed, 1)
            dve.wait_ge(w_summed, 1)
            nc.vector.tensor_reduce(w_row[:], w_sum[:], AX.X, ALU.add).then_inc(w_summed, 1)
            for l in range(LAYERS):
                dve.wait_ge(w_hi_ready, l + 1)
                nc.vector.tensor_tensor(wt_lo[:, l], z_ps[:, l, 0, 0:C], wt_hi[:, l].bitcast(F32),
                                        ALU.subtract).then_inc(w_ready, 1)
            dve.wait_ge(w_summed, 2)

            LINKS = (7, 5)

            class Chain:

                def __init__(s, l, n):
                    s.l, s.at = l, LINKS[l] * n

                def link(s, instruction):
                    s.at = s.at + 1
                    instruction.then_inc(chain[s.l], 1)
                    dve.wait_ge(chain[s.l], s.at)

            def bn_quarter0(b, octet, half_of):
                for g in range(half_of * OCTET // 2, (half_of + 1) * OCTET // 2):
                    nc.vector.bn_stats(bn_first[:, bass.ds(OCTET * octet + g, 1)].rearrange("p g s -> p (g s)"),
                                       ring[:, slot(b, 0), :, bass.ds(GW * (OCTET * octet + g), GW)])

            def bn_late(b, octet, q, g):
                return nc.vector.bn_stats(bn_rest[:, g, q - 1],
                                          ring[:, slot(b, q), :, bass.ds(GW * (OCTET * octet + g), GW)])

            def channel_sums0(b, octet):
                n = octets_of(b, octet)
                dve.wait_ge(bn_done, n + 1)
                c = Chain(0, n)
                first = bn_first[:, bass.ds(OCTET * octet, OCTET)].rearrange("p g (r s) -> p g r s", s=3)
                rest = bn_rest[:].rearrange("p g q (r s) -> p g (q r) s", s=3)
                means = ((first[:, :, :, 1], slice(0, 2)), (rest[:, :, :, 1], slice(2, 2 * QUARTERS)))
                for m, to in means:
                    last = nc.vector.tensor_tensor(mean_sq[:, :, to], m, m, ALU.mult)
                c.link(last)
                for m2, to in ((first[:, :, :, 2], slice(0, 2)), (rest[:, :, :, 2], slice(2, 2 * QUARTERS))):
                    last = nc.vector.scalar_tensor_tensor(out=sq_sum[:, :, to], in0=mean_sq[:, :, to], scalar=float(HALF),
                                                          in1=m2, op0=ALU.mult, op1=ALU.add)
                c.link(last)
                nc.vector.tensor_reduce(parts[0][:, 1, bass.ds(OCTET * octet, OCTET)], sq_sum[:], AX.X, ALU.add)
                nc.vector.tensor_reduce(mean[:, 0], first[:, :, :, 1], AX.X, ALU.add)
                c.link(nc.vector.tensor_reduce(tmp[:, 0], rest[:, :, :, 1], AX.X, ALU.add))
                nc.vector.tensor_tensor(parts[0][:, 0, bass.ds(OCTET * octet, OCTET)], mean[:, 0], tmp[:, 0],
                                        ALU.add).then_inc(parts_ready[0], 1)

            def channel_sums1(b, octet):
                n = octets_of(b, octet)
                of = bass.ds(OCTET * octet, OCTET)
                dve.wait_ge(parts_ready[0], n + 1)
                dve.wait_ge(y_ready, 2 * (STEPS * b + STEPS0 * (octet + 1)))
                dve.wait_ge(squared, 2 * STEPS0 * (n + 1))
                c = Chain(1, n)
                nc.vector.tensor_tensor(parts[1][:, 1, of], x2_sum[:, 0, of], x2_sum[:, 1, of], ALU.add)
                c.link(nc.vector.tensor_tensor(tmp[:, 1], y_sum[:, 0, of], y_sum[:, 1, of], ALU.add))
                nc.vector.scalar_tensor_tensor(out=parts[1][:, 0, of], in0=parts[0][:, 0, of], scalar=float(HALF),
                                               in1=tmp[:, 1], op0=ALU.mult, op1=ALU.add).then_inc(parts_ready[1], 1)

            def read_stats(l, n):
                dve.wait_ge(stat_ready[l], n + 1)
                nc.vector.tensor_scalar(mean[:, l], stat_ps[:, 0:OCTET], (HALF if l == 0 else 1) / COUNT, None, ALU.mult)
                nc.vector.tensor_scalar(ex2[:, l], stat_ps[:, OCTET:2 * OCTET], 1.0 / COUNT, None,
                                        ALU.mult).then_inc(stat_read[l], 1)

            def coefficients(l, octet, n):
                of = bass.ds(OCTET * octet, OCTET)
                dve.wait_ge(stat_read[l], n + 1)
                c = Chain(l, n)
                c.at = c.at + (3 if l == 0 else 1)
                c.link(nc.vector.tensor_tensor(tmp[:, l], mean[:, l], mean[:, l], ALU.mult))
                c.link(nc.vector.tensor_tensor(var[:, l], ex2[:, l], tmp[:, l], ALU.subtract))
                nc.vector.tensor_scalar(var[:, l], var[:, l], 0.0, EPS, ALU.max, ALU.add).then_inc(var_ready[l], 1)
                dve.wait_ge(var_ready[l], n + 1)
                c.link(nc.vector.reciprocal(inv_var[:, l, of], var[:, l]))
                nc.vector.scalar_tensor_tensor(out=s_bias[:, l, of], in0=mean[:, l], scalar=-float(C),
                                               in1=inv_var[:, l, of], op0=ALU.mult, op1=ALU.mult).then_inc(coef_ready[l], 1)
                nc.vector.tensor_scalar(tmp[:, l], mean[:, l], w_row[:, l:l + 1], None,
                                        ALU.mult).then_inc(chain[l], 1)

            def offsets(l, octet, n):
                of = bass.ds(OCTET * octet, OCTET)
                dve.wait_ge(std_ready[l], n + 1)
                dve.wait_ge(chain[l], LINKS[l] * (n + 1))
                nc.vector.scalar_tensor_tensor(out=beta[:, l, of], in0=std[:, l], scalar=b_sum[:, l:l + 1],
                                               in1=tmp[:, l], op0=ALU.mult, op1=ALU.subtract).then_inc(beta_ready[l], 1)

            def multiply(st, a):
                u = 2 * st.t + a
                dve.wait_ge(s_ready, u + 1)
                dve.wait_ge(prod_ready, u + 1)
                g = bass.ds(st.group + a, 1)
                nc.vector.scalar_tensor_tensor(out=z_ps[:, a, :, 0:PIX], in0=z_ps[:, a, :, 0:PIX],
                                               scalar=beta[:, st.layer, g], in1=s_sb[:, a], op0=ALU.add, op1=ALU.mult,
                                               accum_out=None if st.layer else y_sum[:, st.half, g]).then_inc(y_ready, 1)

            def add(st, a):
                dve.wait_ge(y_ready, 2 * st.t + a + 1)
                xs = columns(st, GW, a)
                nc.vector.tensor_tensor(xs, z_ps[:, a, :, 0:PIX].rearrange("p q (h w) -> p q h w", w=GW), xs,
                                        ALU.add).then_inc(added, 1)

            def section(layer, half, o, octet, before):
                b = image
                dve.wait_ge(beta_ready[layer], octets_of(b, octet) + 1)
                ends = [(l, k, octet + rel if layer == 0 else OCTETS - 1) for l, rel, k in finishes(layer, half, o)]
                for st in steps(b, layer, half, octet):
                    for l, k, of in ends:
                        if st.k == k - 1:
                            (channel_sums1 if l else channel_sums0)(b, of)
                    multiply(st, 0)
                    add(st, 0)
                    multiply(st, 1)
                    for l, k, of in ends:
                        if st.k == k - 1:
                            read_stats(l, octets_of(b, of))
                    add(st, 1)
                    for l, k, of in ends:
                        if st.k == k - 1:
                            coefficients(l, of, octets_of(b, of))
                        if st.k == min(k + 1, 3 if layer else 7):
                            offsets(l, of, octets_of(b, of))
                    if layer == 0 and o != OCTETS - 1 and st.k < 4:
                        for g in (2 * st.k, 2 * st.k + 1):
                            for q in range(1, QUARTERS):
                                last = bn_late(b, octet + 1, q, g)
                        if st.k == 3:
                            last.then_inc(bn_done, 1)
                    if (layer, half) == (1, 0) and st.k < 2 and b + 1 < B:
                        if st.k == 0:
                            dve.wait_ge(loaded[0], 16 * (b + 2))
                        bn_quarter0(b + 1, octet, st.k)

            for image in range(B):
                if image == 0:
                    dve.wait_ge(loaded[0], 16)
                    with dve.Fori(0, OCTETS) as octet:
                        for j in range(2):
                            bn_quarter0(0, octet, j)
                for q in range(1, QUARTERS):
                    dve.wait_ge(loaded[q], 16 * (image + 1))
                    for g in range(OCTET):
                        last = bn_late(image, 0, q, g)
                last.then_inc(bn_done, 1)
                channel_sums0(image, 0)
                read_stats(0, octets_of(image, 0))
                coefficients(0, 0, octets_of(image, 0))
                offsets(0, 0, octets_of(image, 0))
                sections(dve, image, section)


def kernel(x, L0_conv_offsets, L0_conv_tumor_center, L0_conv_kernel_w, L0_conv_kernel_b,
           L1_conv_offsets, L1_conv_tumor_center, L1_conv_kernel_w, L1_conv_kernel_b):
    import numpy as np
    import concourse.bacc as bacc
    from concourse.bass_utils import run_bass_kernel_spmd

    nc = bacc.Bacc("TRN2", target_bir_lowering=False, num_devices=1, dynamic_dma_scratch_size=4096)
    given = {"x": x, "w0": L0_conv_kernel_w, "b0": L0_conv_kernel_b, "w1": L1_conv_kernel_w, "b1": L1_conv_kernel_b}
    arrays = {n: np.ascontiguousarray(a) for n, a in given.items()}
    aps = [nc.dram_tensor(n, a.shape, mybir.dt.from_np(a.dtype), kind="ExternalInput").ap() for n, a in arrays.items()]
    out = nc.dram_tensor("out", arrays["x"].shape, mybir.dt.from_np(arrays["x"].dtype), kind="ExternalOutput").ap()
    build(nc, *aps, out)
    return run_bass_kernel_spmd(nc, [arrays], core_ids=[0]).results[0]["out"]
```

```python
from contextlib import ExitStack

import concourse.bass as bass
from concourse import mybir

F32 = mybir.dt.float32
F32R = mybir.dt.float32r
BF16 = mybir.dt.bfloat16
ALU = mybir.AluOpType
ACT = mybir.ActivationFunctionType
AX = mybir.AxisListType

C = 128
TAPS = 7
GROUPS = 32
EPS = 1e-5
QUARTERS = 4
SLOTS = 5
OCTET = 8
EARLY = 2
LAYERS = 2


def build(nc, x, w0, b0, w1, b1, out):
    B, _, H, W = x.shape
    ROWS = H // QUARTERS
    GW = W // GROUPS
    PIX = ROWS * GW
    PW = 2 * GW
    COUNT = C * H * GW
    HALF = PIX // 2
    OCTETS = GROUPS // OCTET
    STEPS0 = OCTET
    STEPS1 = OCTET // 4
    STEPS = OCTETS * (STEPS0 + QUARTERS * STEPS1)
    PARTS = ((0, 0), *((1, i) for i in range(QUARTERS)))
    assert PIX <= 512 and (PIX % 2, H % QUARTERS, W % GROUPS) == (0, 0, 0)

    slots, frees, spare = [list(range(QUARTERS))], [], SLOTS - 1
    for b in range(B):
        now = slots[-1]
        upper = sorted((0, 1), key=lambda q: abs(now[q] - spare))
        third = now[upper[1]]
        lower = sorted((2, 3), key=lambda q: abs(now[q] - third))
        frees.append(upper + lower)
        slots.append([spare, now[upper[0]], third, now[lower[0]]])
        spare = now[lower[1]]

    def slot(b, q):
        return slots[b][q]

    class Step:

        def __init__(s, b, layer, part, octet, k):
            s.b, s.layer, s.octet, s.k, s.buf = b, layer, octet, k, k % 2
            s.wide = layer == 1
            if layer == 0:
                s.half, s.pair = k % 2, k // 2
                low, high = sorted((slot(b, 2 * s.half), slot(b, 2 * s.half + 1)))
                s.quarters = slice(low, high + 1, high - low)
                s.t = STEPS * b + STEPS0 * octet + k
            else:
                s.quarter, s.pair = frees[b][part], 2 * k
                s.half = s.quarter // 2
                s.t = STEPS * b + OCTETS * (STEPS0 + STEPS1 * part) + STEPS1 * octet + k
            s.group = OCTET * octet + 2 * s.pair

        def columns(s):
            if s.wide:
                return ring[:, slot(s.b, s.quarter), :, bass.ds(GW * s.group, 2 * PW)]
            return ring[:, s.quarters, :, bass.ds(GW * s.group, PW)]

        def unit(s, a):
            if s.wide:
                return ring[:, slot(s.b, s.quarter), :, bass.ds(GW * s.group + PW * a, PW)].rearrange(
                    "p h (j w) -> p j h w", j=2)
            return ring[:, s.quarters, :, bass.ds(GW * s.group + GW * a, GW)]

        def split(s, x_part):
            if s.wide:
                return x_part[:, s.buf].rearrange("p (h w) -> p h w", w=2 * PW)
            return x_part[:, s.buf].rearrange("p (q h w) -> p q h w", q=2, w=PW)

        def bank(s, x_part, a, j):
            if s.wide:
                return s.split(x_part)[:, :, PW * a + GW * j:PW * a + GW * (j + 1)]
            return s.split(x_part)[:, j, :, GW * a:GW * (a + 1)]

        def groups(s, a):
            if s.wide:
                return [(slice(j, j + 1), bass.ds(s.group + 2 * a + j, 1)) for j in range(2)]
            return [(slice(0, 2), bass.ds(s.group + a, 1))]

    def steps(b, layer, part, octet):
        return [Step(b, layer, part, octet, k) for k in range(STEPS1 if layer else STEPS0)]

    ctx = ExitStack()
    with ctx:
        def sb(name, shape, dt=F32):
            return ctx.enter_context(nc.sbuf_tensor(name, shape, dt))

        def sem(name):
            return ctx.enter_context(nc.semaphore(name))

        ring = sb("ring", [C, SLOTS, ROWS, W])
        x_hi = sb("x_hi", [C, 2, 4 * PIX], F32R)
        x_lo = sb("x_lo", [C, 2, 4 * PIX], F32R)
        s_sb = sb("s_sb", [C, 2, 2, PIX])
        squares = sb("squares", [C, 2, 2 * PIX], BF16)
        bn_first = sb("bn_first", [C, GROUPS, EARLY, 6])
        bn_rest = sb("bn_rest", [C, OCTET, QUARTERS - EARLY, 6])
        mean_sq = sb("mean_sq", [C, OCTET, 2 * QUARTERS])
        sq_sum = sb("sq_sum", [C, OCTET, 2 * QUARTERS])
        parts = [sb(f"parts{l}", [C, 2, GROUPS]) for l in range(LAYERS)]
        y_sum = sb("y_sum", [C, 2, GROUPS])
        x2_sum = sb("x2_sum", [C, 2, GROUPS])
        mean = sb("mean", [C, LAYERS, OCTET])
        ex2 = sb("ex2", [C, LAYERS, OCTET])
        var = sb("var", [C, LAYERS, OCTET])
        std = sb("std", [C, LAYERS, OCTET])
        tmp = sb("tmp", [C, LAYERS, OCTET])
        fine_std = sb("fine_std", [C, LAYERS, OCTET])
        inv_var = sb("inv_var", [C, LAYERS, GROUPS])
        s_bias = sb("s_bias", [C, LAYERS, GROUPS])
        beta = sb("beta", [C, LAYERS, GROUPS])
        wt_hi = sb("wt_hi", [C, LAYERS, C], F32R)
        wt_lo = sb("wt_lo", [C, LAYERS, C], F32R)
        ones = sb("ones", [C, C], F32R)
        w_row = sb("w_row", [C, LAYERS])
        b_sum = sb("b_sum", [C, LAYERS])
        b_half = sb("b_half", [C, LAYERS])
        b_in = sb("b_in", [C, LAYERS, TAPS])
        s_ps = ctx.enter_context(nc.psum_tensor("s_ps", [C, 2, 2, 512], F32))
        z_ps = ctx.enter_context(nc.psum_tensor("z_ps", [C, 2, 2, 512], F32))
        stat_ps = s_ps[:, 1, 0, PIX:PIX + 2 * OCTET]

        prep = ring[:, QUARTERS].rearrange("p h w -> p (h w)")
        w_in = prep[:, 0:LAYERS * TAPS * C].rearrange("p (l n) -> p l n", l=LAYERS)
        w_sum = prep[:, LAYERS * TAPS * C:LAYERS * (TAPS + 1) * C].rearrange("p (l n) -> p l n", l=LAYERS)
        ident = prep[:, LAYERS * (TAPS + 1) * C:LAYERS * (TAPS + 1) * C + C]

        loaded = [sem(f"loaded{q}") for q in range(QUARTERS)]
        stored = [sem(f"stored{q}") for q in range(QUARTERS)]
        waited = sem("waited")
        w_loaded = sem("w_loaded")
        ident_ready = sem("ident_ready")
        ones_ready = sem("ones_ready")
        w_summed = sem("w_summed")
        w_turned = sem("w_turned")
        w_hi_ready = sem("w_hi_ready")
        w_ready = sem("w_ready")
        hi_ready = sem("hi_ready")
        lo_ready = sem("lo_ready")
        sums_ready = sem("sums_ready")
        s_ready = sem("s_ready")
        prod_ready = sem("prod_ready")
        y_ready = sem("y_ready")
        added = sem("added")
        squared = sem("squared")
        bn_done = sem("bn_done")
        chain = [sem(f"chain{l}") for l in range(LAYERS)]
        parts_ready = [sem(f"parts_ready{l}") for l in range(LAYERS)]
        stat_ready = [sem(f"stat_ready{l}") for l in range(LAYERS)]
        stat_read = [sem(f"stat_read{l}") for l in range(LAYERS)]
        var_ready = [sem(f"var_ready{l}") for l in range(LAYERS)]
        std_ready = [sem(f"std_ready{l}") for l in range(LAYERS)]
        coef_ready = [sem(f"coef_ready{l}") for l in range(LAYERS)]
        beta_ready = [sem(f"beta_ready{l}") for l in range(LAYERS)]

        def wait(e, s, value):
            if not (isinstance(value, int) and value <= 0):
                e.wait_ge(s, value)

        def octets_of(b, o):
            return OCTETS * b + o

        def chains(layer, part, o, octet, later):
            if layer == 0:
                return ([(1, octet - 1, 3 + later)] if o != 0 else []) + (
                    [(0, octet + 1, 5 + later)] if o != OCTETS - 1 else [])
            at = STEPS1 - 1 + later
            return [(1, OCTETS - 1, at % STEPS1)] if (part, o) == (0, at // STEPS1) else []

        def sections(e, b, emit):
            before = steps(b - 1, *PARTS[-1], OCTETS - 1)[-2:] if b else [None, None]
            for layer, part in PARTS:
                first = 2 if (layer, part) == (1, 0) else 1
                last = OCTETS - 1 if layer == 0 else OCTETS
                for o in range(first):
                    emit(layer, part, o, o, before)
                    before = steps(b, layer, part, o)[-2:]
                with e.Fori(first, last) as octet:
                    emit(layer, part, None, octet, steps(b, layer, part, octet - 1)[-2:])
                if layer == 0:
                    emit(layer, part, last, last, steps(b, layer, part, last - 1)[-2:])
                before = steps(b, layer, part, OCTETS - 1)[-2:]

        block = ctx.enter_context(nc.Block())

        @block.sync
        def _(sp):
            def load(b, q):
                sp.dma_start(ring[:, slot(b, q)], x[b, :, ROWS * q:ROWS * (q + 1)]).then_inc(loaded[q], 16)

            def store(b, q):
                sp.dma_start(out[b, :, ROWS * q:ROWS * (q + 1)], ring[:, slot(b, q)]).then_inc(stored[q], 16)

            sp.dma_start(w_in[:, 0], w0.rearrange("(o k) c -> o (k c)", k=TAPS)).then_inc(w_loaded, 16)
            sp.dma_start(w_in[:, 1], w1.rearrange("(o k) c -> o (k c)", k=TAPS)).then_inc(w_loaded, 16)
            sp.dma_start(b_in[:, 0], b0.rearrange("(o k) -> o k", k=TAPS)).then_inc(w_loaded, 16)
            sp.dma_start(b_in[:, 1], b1.rearrange("(o k) -> o k", k=TAPS)).then_inc(w_loaded, 16)
            for q in range(QUARTERS):
                load(0, q)
            sp.wait_ge(added, 4)
            load(1, 0)
            for b in range(B):
                for i, q in enumerate(frees[b]):
                    sp.wait_ge(added, 2 * (STEPS * b + OCTETS * (STEPS0 + STEPS1 * (i + 1))))
                    store(b, q)
                    n = b + 1 + (i + 1) // QUARTERS
                    if n < B:
                        sp.wait_ge(stored[q], 16 * (b + 1))
                        load(n, (i + 1) % QUARTERS)
            for q in range(QUARTERS):
                sp.wait_ge(stored[q], 16 * B)

        @block.scalar
        def _(act):
            for l in range(LAYERS):
                act.wait_ge(w_turned, l + 1)
                nc.scalar.activation(wt_hi[:, l], z_ps[:, l, 0, 0:C], ACT.Copy).then_inc(w_hi_ready, 1)

            def split_hi(st):
                if st.layer == 0:
                    if isinstance(st.octet, int) and st.octet == 0 and st.k < 2:
                        for q in (2 * st.half, 2 * st.half + 1):
                            act.wait_ge(loaded[q], 16 * (st.b + 1))
                else:
                    last = Step(st.b, 0, 0, st.octet, 2 * (st.pair + st.wide) + st.half)
                    act.wait_ge(added, 2 * last.t + 2)
                wait(act, prod_ready, 2 * st.t - 2)
                nc.scalar.activation(st.split(x_hi), st.columns(), ACT.Copy).then_inc(hi_ready, 1)

            def scale_sums(st, in_loop=False):
                act.wait_ge(coef_ready[st.layer], octets_of(st.b, st.octet) + 1)
                for a in range(2):
                    act.wait_ge(sums_ready, 2 * st.t + a + 1)
                    wait(act, y_ready, 2 * st.t + a - 1)
                    if in_loop:
                        act.sem_inc(waited, 1)
                    for banks, g in st.groups(a):
                        last = nc.scalar.activation(s_sb[:, a, banks], s_ps[:, a, banks, 0:PIX], ACT.Identity,
                                                    scale=inv_var[:, st.layer, g], bias=s_bias[:, st.layer, g])
                    last.then_inc(s_ready, 1)

            def square(st):
                for a in range(2):
                    act.wait_ge(added, 2 * st.t + a + 1)
                    done = 2 * STEPS0 * octets_of(st.b, st.octet) + 2 * st.k + a
                    wait(act, squared, done - 1)
                    nc.scalar.activation(squares[:, a].rearrange("p (q h w) -> p q h w", q=2, h=ROWS), st.unit(a),
                                         ACT.Square,
                                         accum_out=x2_sum[:, st.half, bass.ds(st.group + a, 1)]).then_inc(squared, 1)

            def root(l, n):
                act.wait_ge(var_ready[l], n + 1)
                nc.scalar.activation(std[:, l], var[:, l], ACT.Sqrt).then_inc(std_ready[l], 1)

            def section(layer, part, o, octet, before):
                b = image
                roots = chains(layer, part, o, octet, 2)
                line = before + steps(b, layer, part, octet)
                for two, one, st in zip(line, line[1:], line[2:]):
                    split_hi(st)
                    if (layer, o, st.k) == (0, 0, 1):
                        root(0, octets_of(b, 0))
                    if one is not None:
                        scale_sums(one, in_loop=o is None)
                    if two is not None and two.layer == 0:
                        square(two)
                    for l, of, k in roots:
                        if st.k == k:
                            root(l, octets_of(b, of))

            for image in range(B):
                sections(act, image, section)
            scale_sums(steps(B - 1, *PARTS[-1], OCTETS - 1)[-1])

        @block.gpsimd
        def _(pool):
            nc.gpsimd.memset(ident, 0.0).then_inc(ident_ready, 1)
            pool.wait_ge(ident_ready, 1)
            nc.gpsimd.affine_select(out=ident, in_=ident, compare_op=ALU.not_equal, fill=1.0, base=0,
                                    pattern=[[-1, C]], channel_multiplier=1).then_inc(ident_ready, 1)

            def split_lo(st):
                pool.wait_ge(hi_ready, st.t + 1)
                wait(pool, prod_ready, 2 * st.t - 2)
                nc.gpsimd.tensor_tensor(st.split(x_lo), st.columns(), st.split(x_hi).bitcast(F32),
                                        ALU.subtract).then_inc(lo_ready, 1)

            def section(layer, part, o, octet, before):
                for st in steps(image, layer, part, octet):
                    split_lo(st)

            for image in range(B):
                sections(pool, image, section)

        @block.tensor
        def _(pe):
            pe.wait_ge(w_summed, 1)
            pe.wait_ge(ident_ready, 2)
            for l in range(LAYERS):
                nc.tensor.transpose(z_ps[:, l, 0, 0:C], w_sum[:, l], ident).then_inc(w_turned, 1)
            pe.wait_ge(w_ready, LAYERS)
            pe.wait_ge(ones_ready, 1)

            def add_channels(l, octet, n, t):
                pe.wait_ge(parts_ready[l], n + 1)
                wait(pe, s_ready, 2 * t)
                nc.tensor.matmul(stat_ps.rearrange("p (j g) -> p j g", j=2), ones[:].bitcast(F32),
                                 parts[l][:, :, bass.ds(OCTET * octet, OCTET)], start=True, stop=True
                                 ).then_inc(stat_ready[l], 1)

            def sums(st, a):
                if a == 0:
                    pe.wait_ge(lo_ready, st.t + 1)
                wait(pe, s_ready, 2 * st.t + a - 1)
                for q in range(2):
                    for part, x_part in enumerate((x_hi, x_lo)):
                        mm = nc.tensor.matmul(s_ps[:, a, q, 0:PIX], ones[:], st.bank(x_part, a, q),
                                              start=(part == 0), stop=(part == 1))
                mm.then_inc(sums_ready, 1)

            def products(st):
                for a in range(2):
                    wait(pe, added, 2 * st.t + a - 1)
                    for n, (wt, x_part) in enumerate(((wt_hi, x_hi), (wt_hi, x_lo), (wt_lo, x_hi))):
                        for q in range(2):
                            mm = nc.tensor.matmul(z_ps[:, a, q, 0:PIX], wt[:, st.layer],
                                                  st.bank(x_part, a, q),
                                                  start=(n == 0), stop=(n == 2))
                    mm.then_inc(prod_ready, 1)

            def section(layer, part, o, octet, before):
                b = image
                for st in steps(b, layer, part, octet):
                    sums(st, 0)
                    if (layer, o, st.k) == (0, 0, 0):
                        add_channels(0, 0, octets_of(b, 0), st.t)
                        pe.wait_ge(stat_read[0], octets_of(b, 0) + 1)
                    for l, of, k in chains(layer, part, o, octet, 1):
                        if st.k == k:
                            pe.wait_ge(stat_read[l], octets_of(b, of) + 1)
                    sums(st, 1)
                    products(st)
                    for l, of, k in chains(layer, part, o, octet, 0):
                        if st.k == k:
                            add_channels(l, of, octets_of(b, of), st.t + 1)

            for image in range(B):
                sections(pe, image, section)

        @block.vector
        def _(dve):
            nc.vector.memset(ones[:].bitcast(F32), 1.0).then_inc(ones_ready, 1)
            dve.wait_ge(w_loaded, 64)
            for l in range(LAYERS):
                nc.vector.tensor_reduce(w_sum[:, l], w_in[:, l].rearrange("p (k c) -> p c k", k=TAPS), AX.X, ALU.add)
            nc.vector.tensor_reduce(b_sum[:], b_in[:], AX.X, ALU.add).then_inc(w_summed, 1)
            dve.wait_ge(w_summed, 1)
            nc.vector.tensor_scalar(b_half[:], b_sum[:], 0.5, None, ALU.mult)
            nc.vector.tensor_reduce(w_row[:], w_sum[:], AX.X, ALU.add).then_inc(w_summed, 1)
            for l in range(LAYERS):
                dve.wait_ge(w_hi_ready, l + 1)
                nc.vector.tensor_tensor(wt_lo[:, l], z_ps[:, l, 0, 0:C], wt_hi[:, l].bitcast(F32),
                                        ALU.subtract).then_inc(w_ready, 1)
            dve.wait_ge(w_summed, 2)

            SUMS = (3, 1)
            LINKS = (SUMS[0] + 7, SUMS[1] + 7)

            def bn_early(b, octet, q, lot, size):
                for g in range(size * lot, size * (lot + 1)):
                    nc.vector.bn_stats(bn_first[:, bass.ds(OCTET * octet + g, 1), q].rearrange("p g s -> p (g s)"),
                                       ring[:, slot(b, q), :, bass.ds(GW * (OCTET * octet + g), GW)])

            def bn_late(b, octet, q, g):
                return nc.vector.bn_stats(bn_rest[:, g, q - EARLY],
                                          ring[:, slot(b, q), :, bass.ds(GW * (OCTET * octet + g), GW)])

            def link(l, n, count):
                dve.wait_ge(chain[l], LINKS[l] * n + count)

            def channel_sums0(b, octet, i):
                n = octets_of(b, octet)
                of = bass.ds(OCTET * octet, OCTET)
                first = bn_first[:, of].rearrange("p g q (r s) -> p g (q r) s", s=3)
                rest = bn_rest[:].rearrange("p g q (r s) -> p g (q r) s", s=3)
                both = ((first, slice(0, 2 * EARLY)), (rest, slice(2 * EARLY, 2 * QUARTERS)))
                if i == 0:
                    dve.wait_ge(bn_done, n + 1)
                    for bn, to in both:
                        last = nc.vector.tensor_tensor(mean_sq[:, :, to], bn[:, :, :, 1], bn[:, :, :, 1], ALU.mult)
                    last.then_inc(chain[0], 1)
                if i == 1:
                    link(0, n, 1)
                    for bn, to in both:
                        last = nc.vector.scalar_tensor_tensor(out=sq_sum[:, :, to], in0=mean_sq[:, :, to],
                                                              scalar=float(HALF), in1=bn[:, :, :, 2],
                                                              op0=ALU.mult, op1=ALU.add)
                    last.then_inc(chain[0], 1)
                if i == 2:
                    link(0, n, 2)
                    nc.vector.tensor_reduce(parts[0][:, 1, of], sq_sum[:], AX.X, ALU.add)
                    nc.vector.tensor_reduce(mean[:, 0], first[:, :, :, 1], AX.X, ALU.add)
                    nc.vector.tensor_reduce(tmp[:, 0], rest[:, :, :, 1], AX.X, ALU.add).then_inc(chain[0], 1)
                if i == 3:
                    link(0, n, 3)
                    nc.vector.tensor_tensor(parts[0][:, 0, of], mean[:, 0], tmp[:, 0], ALU.add).then_inc(parts_ready[0], 1)

            def channel_sums1(b, octet, i):
                n = octets_of(b, octet)
                of = bass.ds(OCTET * octet, OCTET)
                if i == 2:
                    dve.wait_ge(parts_ready[0], n + 1)
                    dve.wait_ge(y_ready, 2 * (STEPS * b + STEPS0 * (octet + 1)))
                    dve.wait_ge(squared, 2 * STEPS0 * (n + 1))
                    nc.vector.tensor_tensor(parts[1][:, 1, of], x2_sum[:, 0, of], x2_sum[:, 1, of], ALU.add)
                    nc.vector.tensor_tensor(tmp[:, 1], y_sum[:, 0, of], y_sum[:, 1, of], ALU.add).then_inc(chain[1], 1)
                if i == 3:
                    link(1, n, 1)
                    nc.vector.scalar_tensor_tensor(out=parts[1][:, 0, of], in0=parts[0][:, 0, of], scalar=float(HALF),
                                                   in1=tmp[:, 1], op0=ALU.mult, op1=ALU.add).then_inc(parts_ready[1], 1)

            def read_stats(l, n):
                dve.wait_ge(stat_ready[l], n + 1)
                nc.vector.tensor_scalar(mean[:, l], stat_ps[:, 0:OCTET], (HALF if l == 0 else 1) / COUNT, None, ALU.mult)
                nc.vector.tensor_scalar(ex2[:, l], stat_ps[:, OCTET:2 * OCTET], 1.0 / COUNT, None,
                                        ALU.mult).then_inc(stat_read[l], 1)

            def coefficients(l, octet, n, i):
                of = bass.ds(OCTET * octet, OCTET)
                if i == 0:
                    dve.wait_ge(stat_read[l], n + 1)
                    nc.vector.tensor_tensor(tmp[:, l], mean[:, l], mean[:, l], ALU.mult).then_inc(chain[l], 1)
                if i == 1:
                    link(l, n, SUMS[l] + 1)
                    nc.vector.tensor_tensor(var[:, l], ex2[:, l], tmp[:, l], ALU.subtract).then_inc(chain[l], 1)
                if i == 2:
                    link(l, n, SUMS[l] + 2)
                    nc.vector.tensor_scalar(var[:, l], var[:, l], 0.0, EPS, ALU.max, ALU.add).then_inc(var_ready[l], 1)
                if i == 3:
                    dve.wait_ge(var_ready[l], n + 1)
                    nc.vector.reciprocal(inv_var[:, l, of], var[:, l]).then_inc(chain[l], 1)
                if i == 4:
                    link(l, n, SUMS[l] + 3)
                    nc.vector.scalar_tensor_tensor(out=s_bias[:, l, of], in0=mean[:, l], scalar=-float(C),
                                                   in1=inv_var[:, l, of], op0=ALU.mult,
                                                   op1=ALU.mult).then_inc(coef_ready[l], 1)
                    nc.vector.tensor_scalar(tmp[:, l], mean[:, l], w_row[:, l:l + 1], None,
                                            ALU.mult).then_inc(chain[l], 1)

            def offsets(l, octet, n, i):
                if i == 0:
                    dve.wait_ge(std_ready[l], n + 1)
                    nc.vector.reciprocal(fine_std[:, l], std[:, l]).then_inc(chain[l], 1)
                if i == 1:
                    link(l, n, SUMS[l] + 5)
                    nc.vector.tensor_tensor(fine_std[:, l], fine_std[:, l], var[:, l], ALU.mult).then_inc(chain[l], 1)
                if i == 2:
                    link(l, n, SUMS[l] + 6)
                    nc.vector.tensor_tensor(fine_std[:, l], fine_std[:, l], std[:, l], ALU.add).then_inc(chain[l], 1)
                if i == 3:
                    link(l, n, SUMS[l] + 7)
                    nc.vector.scalar_tensor_tensor(out=beta[:, l, bass.ds(OCTET * octet, OCTET)], in0=fine_std[:, l],
                                                   scalar=b_half[:, l:l + 1], in1=tmp[:, l], op0=ALU.mult,
                                                   op1=ALU.subtract).then_inc(beta_ready[l], 1)

            def small(b, l, octet, later, i):
                n = octets_of(b, octet)
                if later == -1:
                    (channel_sums1 if l else channel_sums0)(b, octet, i)
                if later == 0 and i == 0:
                    read_stats(l, n)
                if later == 0 and i > 0:
                    coefficients(l, octet, n, i - 1)
                if later == 1 and i < 2:
                    coefficients(l, octet, n, 3 + i)
                if later == 2:
                    offsets(l, octet, n, i)

            def multiply(st, a):
                u = 2 * st.t + a
                dve.wait_ge(s_ready, u + 1)
                dve.wait_ge(prod_ready, u + 1)
                for banks, g in st.groups(a):
                    last = nc.vector.scalar_tensor_tensor(
                        out=z_ps[:, a, banks, 0:PIX], in0=z_ps[:, a, banks, 0:PIX], scalar=beta[:, st.layer, g],
                        in1=s_sb[:, a, banks], op0=ALU.add, op1=ALU.mult,
                        accum_out=None if st.layer else y_sum[:, st.half, g])
                last.then_inc(y_ready, 1)

            def add(st, a):
                dve.wait_ge(y_ready, 2 * st.t + a + 1)
                xs = st.unit(a)
                nc.vector.tensor_tensor(xs, z_ps[:, a, :, 0:PIX].rearrange("p q (h w) -> p q h w", w=GW), xs,
                                        ALU.add).then_inc(added, 1)

            def section(layer, part, o, octet, before):
                b = image
                dve.wait_ge(beta_ready[layer], octets_of(b, octet) + 1)
                for st in steps(b, layer, part, octet):
                    due = [(l, of, later) for later in range(-1, 3)
                           for l, of, k in chains(layer, part, o, octet, later) if k == st.k]
                    for i, (large, a) in enumerate(((multiply, 0), (multiply, 1), (add, 0), (add, 1))):
                        large(st, a)
                        for l, of, later in due:
                            small(b, l, of, later, i)
                    if layer == 0 and o != OCTETS - 1 and st.k < 4:
                        late = [(q, g) for g in range(OCTET) for q in range(EARLY, QUARTERS)]
                        each = len(late) // 4
                        for q, g in late[each * st.k:each * (st.k + 1)]:
                            last = bn_late(b, octet + 1, q, g)
                        if st.k == 3:
                            last.then_inc(bn_done, 1)
                    if layer == 1 and b + 1 < B:
                        q, second = part // 2, part % 2
                        if (second, o, st.k) == (0, 0, 0):
                            dve.wait_ge(loaded[q], 16 * (b + 2))
                        bn_early(b + 1, octet, q, 2 * second + st.k, OCTET // 4)

            for image in range(B):
                for q in range(EARLY if image == 0 else 0):
                    dve.wait_ge(loaded[q], 16)
                    with dve.Fori(0, OCTETS) as octet:
                        bn_early(0, octet, q, 0, OCTET)
                for q in range(EARLY, QUARTERS):
                    dve.wait_ge(loaded[q], 16 * (image + 1))
                    for g in range(OCTET):
                        last = bn_late(image, 0, q, g)
                last.then_inc(bn_done, 1)
                for later in range(-1, 3):
                    for i in range(4):
                        small(image, 0, 0, later, i)
                sections(dve, image, section)


def kernel(x, L0_conv_offsets, L0_conv_tumor_center, L0_conv_kernel_w, L0_conv_kernel_b,
           L1_conv_offsets, L1_conv_tumor_center, L1_conv_kernel_w, L1_conv_kernel_b):
    import numpy as np
    import concourse.bacc as bacc
    from concourse.bass_utils import run_bass_kernel_spmd

    nc = bacc.Bacc("TRN2", target_bir_lowering=False, num_devices=1, dynamic_dma_scratch_size=4096)
    given = {"x": x, "w0": L0_conv_kernel_w, "b0": L0_conv_kernel_b, "w1": L1_conv_kernel_w, "b1": L1_conv_kernel_b}
    arrays = {n: np.ascontiguousarray(a) for n, a in given.items()}
    aps = [nc.dram_tensor(n, a.shape, mybir.dt.from_np(a.dtype), kind="ExternalInput").ap() for n, a in arrays.items()]
    out = nc.dram_tensor("out", arrays["x"].shape, mybir.dt.from_np(arrays["x"].dtype), kind="ExternalOutput").ap()
    build(nc, *aps, out)
    return run_bass_kernel_spmd(nc, [arrays], core_ids=[0]).results[0]["out"]
```

```python
from contextlib import ExitStack

import concourse.bass as bass
from concourse import mybir

F32 = mybir.dt.float32
F32R = mybir.dt.float32r
BF16 = mybir.dt.bfloat16
ALU = mybir.AluOpType
ACT = mybir.ActivationFunctionType
AX = mybir.AxisListType

C = 128
TAPS = 7
GROUPS = 32
EPS = 1e-5
QUARTERS = 4
SLOTS = 5
OCTET = 8
EARLY = 2
LAYERS = 2


def build(nc, x, w0, b0, w1, b1, out):
    B, _, H, W = x.shape
    ROWS = H // QUARTERS
    GW = W // GROUPS
    PIX = ROWS * GW
    PW = 2 * GW
    COUNT = C * H * GW
    HALF = PIX // 2
    OCTETS = GROUPS // OCTET
    STEPS0 = OCTET
    STEPS1 = OCTET // 4
    STEPS = OCTETS * (STEPS0 + QUARTERS * STEPS1)
    PARTS = ((0, 0), *((1, i) for i in range(QUARTERS)))
    assert PIX <= 512 and (PIX % 2, H % QUARTERS, W % GROUPS) == (0, 0, 0)

    slots, frees, spare = [list(range(QUARTERS))], [], SLOTS - 1
    for b in range(B):
        now = slots[-1]
        upper = sorted((0, 1), key=lambda q: abs(now[q] - spare))
        third = now[upper[1]]
        lower = sorted((2, 3), key=lambda q: abs(now[q] - third))
        frees.append(upper + lower)
        slots.append([spare, now[upper[0]], third, now[lower[0]]])
        spare = now[lower[1]]

    def slot(b, q):
        return slots[b][q]

    class Step:

        def __init__(s, b, layer, part, octet, k):
            s.b, s.layer, s.octet, s.k, s.buf = b, layer, octet, k, k % 2
            s.wide = layer == 1
            if layer == 0:
                s.half, s.pair = k % 2, k // 2
                low, high = sorted((slot(b, 2 * s.half), slot(b, 2 * s.half + 1)))
                s.quarters = slice(low, high + 1, high - low)
                s.t = STEPS * b + STEPS0 * octet + k
            else:
                s.quarter, s.pair = frees[b][part], 2 * k
                s.half = s.quarter // 2
                s.t = STEPS * b + OCTETS * (STEPS0 + STEPS1 * part) + STEPS1 * octet + k
            s.group = OCTET * octet + 2 * s.pair

        def columns(s):
            if s.wide:
                return ring[:, slot(s.b, s.quarter), :, bass.ds(GW * s.group, 2 * PW)]
            return ring[:, s.quarters, :, bass.ds(GW * s.group, PW)]

        def unit(s, a):
            if s.wide:
                return ring[:, slot(s.b, s.quarter), :, bass.ds(GW * s.group + PW * a, PW)].rearrange(
                    "p h (j w) -> p j h w", j=2)
            return ring[:, s.quarters, :, bass.ds(GW * s.group + GW * a, GW)]

        def split(s, x_part):
            if s.wide:
                return x_part[:, s.buf].rearrange("p (h w) -> p h w", w=2 * PW)
            return x_part[:, s.buf].rearrange("p (q h w) -> p q h w", q=2, w=PW)

        def bank(s, x_part, a, j):
            if s.wide:
                return s.split(x_part)[:, :, PW * a + GW * j:PW * a + GW * (j + 1)]
            return s.split(x_part)[:, j, :, GW * a:GW * (a + 1)]

        def groups(s, a):
            if s.wide:
                return [(slice(j, j + 1), bass.ds(s.group + 2 * a + j, 1)) for j in range(2)]
            return [(slice(0, 2), bass.ds(s.group + a, 1))]

    def steps(b, layer, part, octet):
        return [Step(b, layer, part, octet, k) for k in range(STEPS1 if layer else STEPS0)]

    ctx = ExitStack()
    with ctx:
        def sb(name, shape, dt=F32):
            return ctx.enter_context(nc.sbuf_tensor(name, shape, dt))

        def sem(name):
            return ctx.enter_context(nc.semaphore(name))

        ring = sb("ring", [C, SLOTS, ROWS, W])
        x_hi = sb("x_hi", [C, 2, 4 * PIX], F32R)
        x_lo = sb("x_lo", [C, 2, 4 * PIX], F32R)
        s_sb = sb("s_sb", [C, 2, 2, PIX])
        squares = sb("squares", [C, 2, 2 * PIX], BF16)
        bn = sb("bn", [C, GROUPS, QUARTERS, 6])
        mean_sq = sb("mean_sq", [C, OCTET, 2 * QUARTERS])
        sq_sum = sb("sq_sum", [C, OCTET, 2 * QUARTERS])
        parts = [sb(f"parts{l}", [C, 2, GROUPS]) for l in range(LAYERS)]
        y_x2_sum = sb("y_x2_sum", [C, 2, 2, GROUPS])
        y_sum, x2_sum = y_x2_sum[:, 0], y_x2_sum[:, 1]
        mean = sb("mean", [C, LAYERS, OCTET])
        ex2 = sb("ex2", [C, LAYERS, OCTET])
        var = sb("var", [C, LAYERS, OCTET])
        std = sb("std", [C, LAYERS, OCTET])
        tmp = sb("tmp", [C, LAYERS, OCTET])
        fine_std = sb("fine_std", [C, LAYERS, OCTET])
        inv_var = sb("inv_var", [C, LAYERS, GROUPS])
        s_bias = sb("s_bias", [C, LAYERS, GROUPS])
        beta = sb("beta", [C, LAYERS, GROUPS])
        wt_hi = sb("wt_hi", [C, LAYERS, C], F32R)
        wt_lo = sb("wt_lo", [C, LAYERS, C], F32R)
        ones = sb("ones", [C, C], F32R)
        w_row = sb("w_row", [C, LAYERS])
        b_sum = sb("b_sum", [C, LAYERS])
        b_half = sb("b_half", [C, LAYERS])
        b_in = sb("b_in", [C, LAYERS, TAPS])
        s_ps = ctx.enter_context(nc.psum_tensor("s_ps", [C, 2, 2, 512], F32))
        z_ps = ctx.enter_context(nc.psum_tensor("z_ps", [C, 2, 2, 512], F32))
        stat_ps = s_ps[:, 1, 0, PIX:PIX + 2 * OCTET]

        prep = ring[:, QUARTERS].rearrange("p h w -> p (h w)")
        w_in = prep[:, 0:LAYERS * TAPS * C].rearrange("p (l n) -> p l n", l=LAYERS)
        w_sum = prep[:, LAYERS * TAPS * C:LAYERS * (TAPS + 1) * C].rearrange("p (l n) -> p l n", l=LAYERS)
        ident = prep[:, LAYERS * (TAPS + 1) * C:LAYERS * (TAPS + 1) * C + C]

        loaded = [sem(f"loaded{q}") for q in range(QUARTERS)]
        stored = [sem(f"stored{q}") for q in range(QUARTERS)]
        waited = sem("waited")
        rest_loaded = [sem(f"rest_loaded{q}") for q in range(QUARTERS)]
        w_loaded = sem("w_loaded")
        ident_ready = sem("ident_ready")
        ones_ready = sem("ones_ready")
        w_summed = sem("w_summed")
        w_turned = sem("w_turned")
        w_hi_ready = sem("w_hi_ready")
        w_ready = sem("w_ready")
        hi_ready = sem("hi_ready")
        lo_ready = sem("lo_ready")
        sums_ready = sem("sums_ready")
        s_ready = sem("s_ready")
        prod_ready = sem("prod_ready")
        y_ready = sem("y_ready")
        added = sem("added")
        squared = sem("squared")
        bn_done = sem("bn_done")
        chain = [sem(f"chain{l}") for l in range(LAYERS)]
        parts_ready = [sem(f"parts_ready{l}") for l in range(LAYERS)]
        stat_ready = [sem(f"stat_ready{l}") for l in range(LAYERS)]
        stat_read = [sem(f"stat_read{l}") for l in range(LAYERS)]
        var_ready = [sem(f"var_ready{l}") for l in range(LAYERS)]
        std_ready = [sem(f"std_ready{l}") for l in range(LAYERS)]
        coef_ready = [sem(f"coef_ready{l}") for l in range(LAYERS)]
        beta_ready = [sem(f"beta_ready{l}") for l in range(LAYERS)]

        def wait(e, s, value):
            if not (isinstance(value, int) and value <= 0):
                e.wait_ge(s, value)

        def octets_of(b, o):
            return OCTETS * b + o

        def chains(layer, part, o, octet, later):
            if layer == 0:
                return ([(1, octet - 1, 3 + later)] if o != 0 else []) + (
                    [(0, octet + 1, 5 + later)] if o != OCTETS - 1 else [])
            at = STEPS1 - 1 + later
            return [(1, OCTETS - 1, at % STEPS1)] if (part, o) == (0, at // STEPS1) else []

        def sections(e, b, emit):
            before = steps(b - 1, *PARTS[-1], OCTETS - 1)[-2:] if b else [None, None]
            for layer, part in PARTS:
                first = 2 if (layer, part) == (1, 0) else 1
                last = OCTETS - 1 if layer == 0 else OCTETS
                for o in range(first):
                    emit(layer, part, o, o, before)
                    before = steps(b, layer, part, o)[-2:]
                with e.Fori(first, last) as octet:
                    emit(layer, part, None, octet, steps(b, layer, part, octet - 1)[-2:])
                if layer == 0:
                    emit(layer, part, last, last, steps(b, layer, part, last - 1)[-2:])
                before = steps(b, layer, part, OCTETS - 1)[-2:]

        block = ctx.enter_context(nc.Block())

        @block.sync
        def _(sp):
            def load(b, q):
                sp.dma_start(ring[:, slot(b, q)], x[b, :, ROWS * q:ROWS * (q + 1)]).then_inc(loaded[q], 16)

            def store(b, q):
                sp.dma_start(out[b, :, ROWS * q:ROWS * (q + 1)], ring[:, slot(b, q)]).then_inc(stored[q], 16)

            sp.dma_start(w_in[:, 0], w0.rearrange("(o k) c -> o (k c)", k=TAPS)).then_inc(w_loaded, 16)
            sp.dma_start(w_in[:, 1], w1.rearrange("(o k) c -> o (k c)", k=TAPS)).then_inc(w_loaded, 16)
            sp.dma_start(b_in[:, 0], b0.rearrange("(o k) -> o k", k=TAPS)).then_inc(w_loaded, 16)
            sp.dma_start(b_in[:, 1], b1.rearrange("(o k) -> o k", k=TAPS)).then_inc(w_loaded, 16)
            most, last = slice(0, W - GW * OCTET), slice(W - GW * OCTET, W)
            for to, columns in ((loaded, most), (rest_loaded, last)):
                for q in range(QUARTERS):
                    sp.dma_start(ring[:, slot(0, q), :, columns],
                                 x[0, :, ROWS * q:ROWS * (q + 1), columns]).then_inc(to[q], 16)
            sp.wait_ge(added, 4)
            load(1, 0)
            for b in range(B):
                for i, q in enumerate(frees[b]):
                    if (b, i) == (B - 1, QUARTERS - 1):
                        for done, columns in ((STEPS * B - STEPS1, most), (STEPS * B, last)):
                            sp.wait_ge(added, 2 * done)
                            sp.dma_start(out[b, :, ROWS * q:ROWS * (q + 1), columns],
                                         ring[:, slot(b, q), :, columns]).then_inc(stored[q], 16)
                        continue
                    sp.wait_ge(added, 2 * (STEPS * b + OCTETS * (STEPS0 + STEPS1 * (i + 1))))
                    store(b, q)
                    n = b + 1 + (i + 1) // QUARTERS
                    if n < B:
                        sp.wait_ge(stored[q], 16 * (b + 1))
                        load(n, (i + 1) % QUARTERS)
            for q in range(QUARTERS):
                sp.wait_ge(stored[q], 16 * (B + 1 if q == frees[B - 1][-1] else B))

        @block.scalar
        def _(act):
            for l in range(LAYERS):
                act.wait_ge(w_turned, l + 1)
                nc.scalar.activation(wt_hi[:, l], z_ps[:, l, 0, 0:C], ACT.Copy).then_inc(w_hi_ready, 1)

            def split_hi(st):
                if st.layer == 0:
                    if isinstance(st.octet, int) and st.octet == 0 and st.k < 2:
                        for q in (2 * st.half, 2 * st.half + 1):
                            act.wait_ge(loaded[q], 16 * (st.b + 1))
                    if st.b == 0 and isinstance(st.octet, int) and st.octet == OCTETS - 1 and st.k < 2:
                        for q in (2 * st.half, 2 * st.half + 1):
                            act.wait_ge(rest_loaded[q], 16)
                else:
                    last = Step(st.b, 0, 0, st.octet, 2 * (st.pair + st.wide) + st.half)
                    act.wait_ge(added, 2 * last.t + 2)
                wait(act, prod_ready, 2 * st.t - 2)
                nc.scalar.activation(st.split(x_hi), st.columns(), ACT.Copy).then_inc(hi_ready, 1)

            def scale_sums(st, in_loop=False):
                act.wait_ge(coef_ready[st.layer], octets_of(st.b, st.octet) + 1)
                for a in range(2):
                    act.wait_ge(sums_ready, 2 * st.t + a + 1)
                    wait(act, y_ready, 2 * st.t + a - 1)
                    if in_loop:
                        act.sem_inc(waited, 1)
                    for banks, g in st.groups(a):
                        last = nc.scalar.activation(s_sb[:, a, banks], s_ps[:, a, banks, 0:PIX], ACT.Identity,
                                                    scale=inv_var[:, st.layer, g], bias=s_bias[:, st.layer, g])
                    last.then_inc(s_ready, 1)

            def square(st):
                for a in range(2):
                    act.wait_ge(added, 2 * st.t + a + 1)
                    done = 2 * STEPS0 * octets_of(st.b, st.octet) + 2 * st.k + a
                    wait(act, squared, done - 1)
                    nc.scalar.activation(squares[:, a].rearrange("p (q h w) -> p q h w", q=2, h=ROWS), st.unit(a),
                                         ACT.Square,
                                         accum_out=x2_sum[:, st.half, bass.ds(st.group + a, 1)]).then_inc(squared, 1)

            def root(l, n):
                act.wait_ge(var_ready[l], n + 1)
                nc.scalar.activation(std[:, l], var[:, l], ACT.Sqrt).then_inc(std_ready[l], 1)

            def section(layer, part, o, octet, before):
                b = image
                roots = chains(layer, part, o, octet, 2)
                line = before + steps(b, layer, part, octet)
                for two, one, st in zip(line, line[1:], line[2:]):
                    split_hi(st)
                    if (layer, o, st.k) == (0, 0, 1):
                        root(0, octets_of(b, 0))
                    if one is not None:
                        scale_sums(one, in_loop=o is None)
                    if two is not None and two.layer == 0:
                        square(two)
                    for l, of, k in roots:
                        if st.k == k:
                            root(l, octets_of(b, of))

            for image in range(B):
                sections(act, image, section)
            scale_sums(steps(B - 1, *PARTS[-1], OCTETS - 1)[-1])

        @block.gpsimd
        def _(pool):
            nc.gpsimd.memset(ident, 0.0).then_inc(ident_ready, 1)
            pool.wait_ge(ident_ready, 1)
            nc.gpsimd.affine_select(out=ident, in_=ident, compare_op=ALU.not_equal, fill=1.0, base=0,
                                    pattern=[[-1, C]], channel_multiplier=1).then_inc(ident_ready, 1)

            def split_lo(st):
                pool.wait_ge(hi_ready, st.t + 1)
                wait(pool, prod_ready, 2 * st.t - 2)
                nc.gpsimd.tensor_tensor(st.split(x_lo), st.columns(), st.split(x_hi).bitcast(F32),
                                        ALU.subtract).then_inc(lo_ready, 1)

            def section(layer, part, o, octet, before):
                for st in steps(image, layer, part, octet):
                    split_lo(st)

            for image in range(B):
                sections(pool, image, section)

        @block.tensor
        def _(pe):
            pe.wait_ge(w_summed, 1)
            pe.wait_ge(ident_ready, 2)
            for l in range(LAYERS):
                nc.tensor.transpose(z_ps[:, l, 0, 0:C], w_sum[:, l], ident).then_inc(w_turned, 1)
            pe.wait_ge(w_ready, LAYERS)
            pe.wait_ge(ones_ready, 1)

            def add_channels(l, octet, n, t):
                pe.wait_ge(parts_ready[l], n + 1)
                wait(pe, s_ready, 2 * t)
                nc.tensor.matmul(stat_ps.rearrange("p (j g) -> p j g", j=2), ones[:].bitcast(F32),
                                 parts[l][:, :, bass.ds(OCTET * octet, OCTET)], start=True, stop=True
                                 ).then_inc(stat_ready[l], 1)

            def sums(st, a):
                if a == 0:
                    pe.wait_ge(lo_ready, st.t + 1)
                wait(pe, s_ready, 2 * st.t + a - 1)
                for q in range(2):
                    for part, x_part in enumerate((x_hi, x_lo)):
                        mm = nc.tensor.matmul(s_ps[:, a, q, 0:PIX], ones[:], st.bank(x_part, a, q),
                                              start=(part == 0), stop=(part == 1))
                mm.then_inc(sums_ready, 1)

            def products(st):
                for a in range(2):
                    wait(pe, added, 2 * st.t + a - 1)
                    for n, (wt, x_part) in enumerate(((wt_hi, x_hi), (wt_hi, x_lo), (wt_lo, x_hi))):
                        for q in range(2):
                            mm = nc.tensor.matmul(z_ps[:, a, q, 0:PIX], wt[:, st.layer],
                                                  st.bank(x_part, a, q),
                                                  start=(n == 0), stop=(n == 2))
                    mm.then_inc(prod_ready, 1)

            def section(layer, part, o, octet, before):
                b = image
                for st in steps(b, layer, part, octet):
                    sums(st, 0)
                    if (layer, o, st.k) == (0, 0, 0):
                        add_channels(0, 0, octets_of(b, 0), st.t)
                        pe.wait_ge(stat_read[0], octets_of(b, 0) + 1)
                    for l, of, k in chains(layer, part, o, octet, 1):
                        if st.k == k:
                            pe.wait_ge(stat_read[l], octets_of(b, of) + 1)
                    sums(st, 1)
                    products(st)
                    for l, of, k in chains(layer, part, o, octet, 0):
                        if st.k == k:
                            add_channels(l, of, octets_of(b, of), st.t + 1)

            for image in range(B):
                sections(pe, image, section)

        @block.vector
        def _(dve):
            nc.vector.memset(ones[:].bitcast(F32), 1.0).then_inc(ones_ready, 1)
            dve.wait_ge(w_loaded, 64)
            for l in range(LAYERS):
                nc.vector.tensor_reduce(w_sum[:, l], w_in[:, l].rearrange("p (k c) -> p c k", k=TAPS), AX.X, ALU.add)
            nc.vector.tensor_reduce(b_sum[:], b_in[:], AX.X, ALU.add).then_inc(w_summed, 1)
            dve.wait_ge(w_summed, 1)
            nc.vector.tensor_scalar(b_half[:], b_sum[:], 0.5, None, ALU.mult)
            nc.vector.tensor_reduce(w_row[:], w_sum[:], AX.X, ALU.add).then_inc(w_summed, 1)
            for l in range(LAYERS):
                dve.wait_ge(w_hi_ready, l + 1)
                nc.vector.tensor_tensor(wt_lo[:, l], z_ps[:, l, 0, 0:C], wt_hi[:, l].bitcast(F32),
                                        ALU.subtract).then_inc(w_ready, 1)
            dve.wait_ge(w_summed, 2)

            SUMS = (2, 1)
            LINKS = (SUMS[0] + 7, SUMS[1] + 7)

            def bn_stats(b, octet, q, g):
                return nc.vector.bn_stats(bn[:, bass.ds(OCTET * octet + g, 1), q].rearrange("p g s -> p (g s)"),
                                          ring[:, slot(b, q), :, bass.ds(GW * (OCTET * octet + g), GW)])

            def link(l, n, count):
                dve.wait_ge(chain[l], LINKS[l] * n + count)

            def channel_sums0(b, octet, i):
                n = octets_of(b, octet)
                of = bass.ds(OCTET * octet, OCTET)
                halves = bn[:, of].rearrange("p g q (r s) -> p g (q r) s", s=3)
                if i == 0:
                    dve.wait_ge(bn_done, n + 1)
                    nc.vector.tensor_tensor(mean_sq[:], halves[:, :, :, 1], halves[:, :, :, 1],
                                            ALU.mult).then_inc(chain[0], 1)
                if i == 1:
                    link(0, n, 1)
                    nc.vector.scalar_tensor_tensor(out=sq_sum[:], in0=mean_sq[:], scalar=float(HALF),
                                                   in1=halves[:, :, :, 2], op0=ALU.mult,
                                                   op1=ALU.add).then_inc(chain[0], 1)
                if i == 2:
                    link(0, n, 2)
                    nc.vector.tensor_reduce(parts[0][:, 1, of], sq_sum[:], AX.X, ALU.add)
                    nc.vector.tensor_reduce(parts[0][:, 0, of], halves[:, :, :, 1], AX.X, ALU.add
                                            ).then_inc(parts_ready[0], 1)

            def channel_sums1(b, octet, i):
                n = octets_of(b, octet)
                of = bass.ds(OCTET * octet, OCTET)
                if i == 2:
                    dve.wait_ge(parts_ready[0], n + 1)
                    dve.wait_ge(y_ready, 2 * (STEPS * b + STEPS0 * (octet + 1)))
                    dve.wait_ge(squared, 2 * STEPS0 * (n + 1))
                    nc.vector.tensor_tensor(parts[1][:, :, of], y_x2_sum[:, :, 0, of], y_x2_sum[:, :, 1, of],
                                            ALU.add).then_inc(chain[1], 1)
                if i == 3:
                    link(1, n, 1)
                    nc.vector.scalar_tensor_tensor(out=parts[1][:, 0, of], in0=parts[0][:, 0, of], scalar=float(HALF),
                                                   in1=parts[1][:, 0, of], op0=ALU.mult,
                                                   op1=ALU.add).then_inc(parts_ready[1], 1)

            def read_stats(l, n):
                dve.wait_ge(stat_ready[l], n + 1)
                nc.vector.tensor_scalar(mean[:, l], stat_ps[:, 0:OCTET], (HALF if l == 0 else 1) / COUNT, None, ALU.mult)
                nc.vector.tensor_scalar(ex2[:, l], stat_ps[:, OCTET:2 * OCTET], 1.0 / COUNT, None,
                                        ALU.mult).then_inc(stat_read[l], 1)

            def coefficients(l, octet, n, i):
                of = bass.ds(OCTET * octet, OCTET)
                if i == 0:
                    dve.wait_ge(stat_read[l], n + 1)
                    nc.vector.tensor_tensor(tmp[:, l], mean[:, l], mean[:, l], ALU.mult).then_inc(chain[l], 1)
                if i == 1:
                    link(l, n, SUMS[l] + 1)
                    nc.vector.tensor_tensor(var[:, l], ex2[:, l], tmp[:, l], ALU.subtract).then_inc(chain[l], 1)
                if i == 2:
                    link(l, n, SUMS[l] + 2)
                    nc.vector.tensor_scalar(var[:, l], var[:, l], 0.0, EPS, ALU.max, ALU.add).then_inc(var_ready[l], 1)
                if i == 3:
                    dve.wait_ge(var_ready[l], n + 1)
                    nc.vector.reciprocal(inv_var[:, l, of], var[:, l]).then_inc(chain[l], 1)
                if i == 4:
                    link(l, n, SUMS[l] + 3)
                    nc.vector.scalar_tensor_tensor(out=s_bias[:, l, of], in0=mean[:, l], scalar=-float(C),
                                                   in1=inv_var[:, l, of], op0=ALU.mult,
                                                   op1=ALU.mult).then_inc(coef_ready[l], 1)
                    nc.vector.tensor_scalar(tmp[:, l], mean[:, l], w_row[:, l:l + 1], None,
                                            ALU.mult).then_inc(chain[l], 1)

            def offsets(l, octet, n, i):
                if i == 0:
                    dve.wait_ge(std_ready[l], n + 1)
                    nc.vector.reciprocal(fine_std[:, l], std[:, l]).then_inc(chain[l], 1)
                if i == 1:
                    link(l, n, SUMS[l] + 5)
                    nc.vector.tensor_tensor(fine_std[:, l], fine_std[:, l], var[:, l], ALU.mult).then_inc(chain[l], 1)
                if i == 2:
                    link(l, n, SUMS[l] + 6)
                    nc.vector.tensor_tensor(fine_std[:, l], fine_std[:, l], std[:, l], ALU.add).then_inc(chain[l], 1)
                if i == 3:
                    link(l, n, SUMS[l] + 7)
                    nc.vector.scalar_tensor_tensor(out=beta[:, l, bass.ds(OCTET * octet, OCTET)], in0=fine_std[:, l],
                                                   scalar=b_half[:, l:l + 1], in1=tmp[:, l], op0=ALU.mult,
                                                   op1=ALU.subtract).then_inc(beta_ready[l], 1)

            def small(b, l, octet, later, i):
                n = octets_of(b, octet)
                if later == -1:
                    (channel_sums1 if l else channel_sums0)(b, octet, i)
                if later == 0 and i == 0:
                    read_stats(l, n)
                if later == 0 and i > 0:
                    coefficients(l, octet, n, i - 1)
                if later == 1 and i < 2:
                    coefficients(l, octet, n, 3 + i)
                if later == 2:
                    offsets(l, octet, n, i)

            def multiply(st, a):
                u = 2 * st.t + a
                dve.wait_ge(s_ready, u + 1)
                dve.wait_ge(prod_ready, u + 1)
                for banks, g in st.groups(a):
                    last = nc.vector.scalar_tensor_tensor(
                        out=z_ps[:, a, banks, 0:PIX], in0=z_ps[:, a, banks, 0:PIX], scalar=beta[:, st.layer, g],
                        in1=s_sb[:, a, banks], op0=ALU.add, op1=ALU.mult,
                        accum_out=None if st.layer else y_sum[:, st.half, g])
                last.then_inc(y_ready, 1)

            def add(st, a):
                dve.wait_ge(y_ready, 2 * st.t + a + 1)
                xs = st.unit(a)
                nc.vector.tensor_tensor(xs, z_ps[:, a, :, 0:PIX].rearrange("p q (h w) -> p q h w", w=GW), xs,
                                        ALU.add).then_inc(added, 1)

            def section(layer, part, o, octet, before):
                b = image
                dve.wait_ge(beta_ready[layer], octets_of(b, octet) + 1)
                for st in steps(b, layer, part, octet):
                    due = [(l, of, later) for later in range(-1, 3)
                           for l, of, k in chains(layer, part, o, octet, later) if k == st.k]
                    stats = []
                    if layer == 0 and o != OCTETS - 1 and st.k < 4:
                        late = [(b, octet + 1, q, g) for q in range(EARLY, QUARTERS) for g in range(OCTET)
                                if (b, o, q) != (0, 0, EARLY)]
                        each = len(late) // 4
                        stats = late[each * st.k:each * (st.k + 1)]
                    if (b, layer, o) == (0, 0, 0) and st.k >= 4:
                        q, second = (st.k - 4) // 2, st.k % 2
                        dve.wait_ge(rest_loaded[q], 16)
                        if st.k == STEPS0 - 1:
                            for late in range(EARLY, QUARTERS):
                                dve.wait_ge(rest_loaded[late], 16)
                        stats = [(0, OCTETS - 1, q, OCTET // 2 * second + g) for g in range(OCTET // 2)]
                    if layer == 1 and b + 1 < B:
                        q, second = part // 2, part % 2
                        if (second, o, st.k) == (0, 0, 0):
                            dve.wait_ge(loaded[q], 16 * (b + 2))
                        first = OCTET // 4 * (2 * second + st.k)
                        stats = [(b + 1, octet, q, first + g) for g in range(OCTET // 4)]
                    if len(stats) == 2:
                        stats = [stats[0], None, stats[1], None]
                    larges = ((multiply, 0), (multiply, 1), (add, 0), (add, 1))
                    if stats:
                        larges = ((multiply, 0), (add, 0), (multiply, 1), (add, 1))
                    for i, (large, a) in enumerate(larges):
                        large(st, a)
                        for l, of, later in due:
                            small(b, l, of, later, i)
                        if stats and stats[i]:
                            last = bn_stats(*stats[i])
                    if layer == 0 and o != OCTETS - 1 and st.k == 3:
                        last.then_inc(bn_done, 1)

            for image in range(B):
                for q in range(EARLY if image == 0 else 0):
                    dve.wait_ge(loaded[q], 16)
                    with dve.Fori(0, OCTETS - 1) as octet:
                        for g in range(OCTET):
                            bn_stats(0, octet, q, g)
                for q in range(EARLY, QUARTERS):
                    dve.wait_ge(loaded[q], 16 * (image + 1))
                    for g in range(OCTET):
                        last = bn_stats(image, 0, q, g)
                    if (image, q) == (0, EARLY):
                        for g in range(OCTET):
                            bn_stats(0, 1, q, g)
                last.then_inc(bn_done, 1)
                for later in range(-1, 3):
                    for i in range(4):
                        small(image, 0, 0, later, i)
                sections(dve, image, section)


def kernel(x, L0_conv_offsets, L0_conv_tumor_center, L0_conv_kernel_w, L0_conv_kernel_b,
           L1_conv_offsets, L1_conv_tumor_center, L1_conv_kernel_w, L1_conv_kernel_b):
    import numpy as np
    import concourse.bacc as bacc
    from concourse.bass_utils import run_bass_kernel_spmd

    nc = bacc.Bacc("TRN2", target_bir_lowering=False, num_devices=1, dynamic_dma_scratch_size=4096)
    given = {"x": x, "w0": L0_conv_kernel_w, "b0": L0_conv_kernel_b, "w1": L1_conv_kernel_w, "b1": L1_conv_kernel_b}
    arrays = {n: np.ascontiguousarray(a) for n, a in given.items()}
    aps = [nc.dram_tensor(n, a.shape, mybir.dt.from_np(a.dtype), kind="ExternalInput").ap() for n, a in arrays.items()]
    out = nc.dram_tensor("out", arrays["x"].shape, mybir.dt.from_np(arrays["x"].dtype), kind="ExternalOutput").ap()
    build(nc, *aps, out)
    return run_bass_kernel_spmd(nc, [arrays], core_ids=[0]).results[0]["out"]
```
